# Optimizing a Trainium2 kernel written in Bass

```python
import numpy as np
import jax
import jax.numpy as jnp

def _softmax(x, axis=-1):
    return jax.nn.softmax(x, axis=axis)

def _gelu(x):
    return jax.nn.gelu(x, approximate=True)

def _silu(x):
    return jax.nn.silu(x)

def _sigmoid(x):
    return jax.nn.sigmoid(x)

def _layernorm(x, axis=-1, eps=1e-05):
    m = jnp.mean(x, axis=axis, keepdims=True)
    v = jnp.var(x, axis=axis, keepdims=True)
    return (x - m) / jnp.sqrt(v + eps)

def _scatter_add(tgt, idx, src, axis=0):
    return tgt.at[idx].add(src)

def _segment_sum(src, seg, n):
    return jax.ops.segment_sum(src, seg, n)
kernel_name = 'mk_cond_resid_d2_seqx_r8_168db9'

def setup_inputs(seed: int=0):
    np.random.seed(seed)
    _w = jnp.asarray

    def _rec_inputs():
        import jax
        import jax.numpy as jnp
        _rk = jax.random.key(seed)
        x = -0.0005207 + 1.001 * jax.random.normal(jax.random.fold_in(_rk, 1), (16, 128, 128), jnp.float32)
        _lenS = 128 - jax.random.randint(jax.random.fold_in(_rk, 7), (16,), 0, max(1, 128 // 4) + 1, jnp.int32)
        _lenS2 = 128 - jax.random.randint(jax.random.fold_in(_rk, 8), (16,), 0, max(1, 128 // 4) + 1, jnp.int32)
        fside_Bx8_0 = jax.random.uniform(jax.random.fold_in(_rk, 11), (16, 8), jnp.float32, 0.0, 0.556406)
        condB_sharedgateprob = jax.random.uniform(jax.random.fold_in(_rk, 12), (16,), jnp.float32, 0.0, 0.794948)
        itok_B_0_8 = jax.random.randint(jax.random.fold_in(_rk, 13), (16,), 0, 9, jnp.int32)
        return (x, fside_Bx8_0, condB_sharedgateprob, itok_B_0_8)
    x, fside_Bx8_0, condB_sharedgateprob, itok_B_0_8 = _rec_inputs()

    def _L0_cond_setup():
        import jax, jax.numpy as jnp
        import numpy as np
        E, B, S, D, F = (8, 2, 128, 128, 512)
        key = jax.random.key(seed)
        ks = jax.random.split(key, 9)
        sc_d = 1.0 / np.sqrt(D)
        sc_f = 1.0 / np.sqrt(F)
        hidden_states = jax.random.normal(ks[0], (B, S, D), dtype=jnp.float32)
        gating_probs = jax.nn.softmax(jax.random.normal(ks[1], (B, E), dtype=jnp.float32), axis=-1)
        shared_gate_prob = jax.nn.sigmoid(jax.random.normal(ks[2], (B, 1), dtype=jnp.float32))
        Wg = jax.random.normal(ks[3], (E, D, F), dtype=jnp.float32) * sc_d
        Wu = jax.random.normal(ks[4], (E, D, F), dtype=jnp.float32) * sc_d
        Wd = jax.random.normal(ks[5], (E, F, D), dtype=jnp.float32) * sc_f
        Sg = jax.random.normal(ks[6], (D, F), dtype=jnp.float32) * sc_d
        Su = jax.random.normal(ks[7], (D, F), dtype=jnp.float32) * sc_d
        Sd = jax.random.normal(ks[8], (F, D), dtype=jnp.float32) * sc_f
        return {'hidden_states': hidden_states, 'gating_probs': gating_probs, 'shared_gate_prob': shared_gate_prob, 'Wg': Wg, 'Wu': Wu, 'Wd': Wd, 'Sg': Sg, 'Su': Su, 'Sd': Sd}
    _L0_cond_all = _L0_cond_setup()
    _L0_cond_in = {k: v for k, v in _L0_cond_all.items() if k in ('Wg', 'Wu', 'Wd', 'Sg', 'Su', 'Sd')}
    del _L0_cond_all

    def _L1_cond_setup():
        import jax, jax.numpy as jnp
        import numpy as np
        LN_EPS = 1e-05
        key = jax.random.key(seed)
        ks = jax.random.split(key, 8)
        B, S, H, A, L = (32, 256, 128, 32, 10)
        return {'hidden_states': jax.random.normal(ks[0], (B, S, H), dtype=jnp.float32), 'language_ids': jax.random.randint(ks[1], (B,), 0, L, dtype=jnp.int64), 'W1': jax.random.normal(ks[2], (L, H, A), dtype=jnp.float32) * (1.0 / np.sqrt(H)), 'b1': jnp.zeros((L, A), dtype=jnp.float32), 'W2': jax.random.normal(ks[3], (L, A, H), dtype=jnp.float32) * (1.0 / np.sqrt(A)), 'b2': jnp.zeros((L, H), dtype=jnp.float32), 'gamma': jnp.ones((L, H), dtype=jnp.float32), 'beta': jnp.zeros((L, H), dtype=jnp.float32)}
    _L1_cond_all = _L1_cond_setup()
    _L1_cond_in = {k: v for k, v in _L1_cond_all.items() if k in ('W1', 'b1', 'W2', 'b2', 'gamma', 'beta')}
    del _L1_cond_all
    return {'x': x, 'fside_Bx8_0': fside_Bx8_0, 'condB_sharedgateprob': condB_sharedgateprob, 'itok_B_0_8': itok_B_0_8, 'L0_cond_Wg': _L0_cond_in['Wg'], 'L0_cond_Wu': _L0_cond_in['Wu'], 'L0_cond_Wd': _L0_cond_in['Wd'], 'L0_cond_Sg': _L0_cond_in['Sg'], 'L0_cond_Su': _L0_cond_in['Su'], 'L0_cond_Sd': _L0_cond_in['Sd'], 'L1_cond_W1': _L1_cond_in['W1'], 'L1_cond_b1': _L1_cond_in['b1'], 'L1_cond_W2': _L1_cond_in['W2'], 'L1_cond_b2': _L1_cond_in['b2'], 'L1_cond_gamma': _L1_cond_in['gamma'], 'L1_cond_beta': _L1_cond_in['beta']}

def reference(x, fside_Bx8_0, condB_sharedgateprob, itok_B_0_8, L0_cond_Wg, L0_cond_Wu, L0_cond_Wd, L0_cond_Sg, L0_cond_Su, L0_cond_Sd, L1_cond_W1, L1_cond_b1, L1_cond_W2, L1_cond_b2, L1_cond_gamma, L1_cond_beta):
    import jax
    import jax.numpy as jnp

    def _L0_cond_ref(hidden_states, gating_probs, shared_gate_prob, Wg, Wu, Wd, Sg, Su, Sd):
        import jax, jax.numpy as jnp
        import numpy as np
        E, B, S, D, F = (8, 2, 128, 128, 512)
        h = hidden_states
        g = jnp.einsum('bsd,edf->ebsf', h, Wg)
        u = jnp.einsum('bsd,edf->ebsf', h, Wu)
        expert_outs = jnp.einsum('ebsf,efd->ebsd', jax.nn.silu(g) * u, Wd)
        expert_output = jnp.einsum('be,ebsd->bsd', gating_probs, expert_outs)
        shared = jnp.einsum('bsf,fd->bsd', jax.nn.silu(h @ Sg) * (h @ Su), Sd)
        sg = shared_gate_prob[:, :, None]
        return (1.0 - sg) * expert_output + sg * shared

    def _L1_cond_ref(hidden_states, language_ids, W1, b1, W2, b2, gamma, beta):
        import jax, jax.numpy as jnp
        import numpy as np
        LN_EPS = 1e-05
        w1 = W1[language_ids]
        w2 = W2[language_ids]
        h = jnp.einsum('bsh,bha->bsa', hidden_states, w1) + b1[language_ids][:, None, :]
        h = jax.nn.relu(h)
        adapted = jnp.einsum('bsa,bah->bsh', h, w2) + b2[language_ids][:, None, :]
        x = hidden_states + adapted
        mean = jnp.mean(x, axis=-1, keepdims=True)
        var = jnp.mean(jnp.square(x - mean), axis=-1, keepdims=True)
        normed = (x - mean) * jax.lax.rsqrt(var + LN_EPS)
        return normed * gamma[language_ids][:, None, :] + beta[language_ids][:, None, :]
    x = x + _L0_cond_ref(x, fside_Bx8_0, condB_sharedgateprob[:, None], L0_cond_Wg, L0_cond_Wu, L0_cond_Wd, L0_cond_Sg, L0_cond_Su, L0_cond_Sd)
    x = x + _L1_cond_ref(x, itok_B_0_8, L1_cond_W1, L1_cond_b1, L1_cond_W2, L1_cond_b2, L1_cond_gamma, L1_cond_beta)
    return x

_drawn_inputs = setup_inputs


def setup_inputs(seed=0):
    import zlib

    import numpy as np

    out = dict(_drawn_inputs(seed))
    spreads = {'L1_cond_b1': (0.0, 0.296),
     'L1_cond_b2': (0.0, 0.1),
     'L1_cond_gamma': (1.0, 0.2),
     'L1_cond_beta': (0.0, 0.1)}
    factors = {}
    for name, (base, spread) in spreads.items():
        noise = np.random.default_rng([zlib.crc32(name.encode()), seed]).standard_normal(out[name].shape)
        drawn = base * np.exp(spread * noise) if base else spread * noise
        out[name] = jnp.asarray(drawn.astype(out[name].dtype))
    for name, factor in factors.items():
        out[name] = (out[name] * factor).astype(out[name].dtype)
    return out
```

```python
from contextlib import ExitStack

import concourse.bass as bass
from concourse import mybir

P = 128
B, S, D = 16, 128, 128
NE, F = 9, 512
CHUNKS = F // P
TILES = 4
BATCHES = B // TILES
N = BATCHES * S
PER_TILE = NE * CHUNKS
A = 32
LANGS = 10
LN_EPS = 1e-5

W_SCALE = 64.0
X_SCALE = 8.0
H_SCALE = 32.0
HIDDEN_RESCALE = H_SCALE / (W_SCALE * X_SCALE)
OUT_RESCALE = 1.0 / (W_SCALE * H_SCALE)

F32 = mybir.dt.float32
F16 = mybir.dt.float16
I32 = mybir.dt.int32
ALU = mybir.AluOpType
ACT = mybir.ActivationFunctionType


def build(nc, xT, weights, gates, shared_gate, language, w1, w2b2, b1, affine, out):
    with ExitStack() as ctx:
        def sb(name, shape, dt):
            return ctx.enter_context(nc.sbuf_tensor(name, shape, dt))

        def bank(name):
            return ctx.enter_context(nc.psum_tensor(name, [P, N], F32))

        def sem(name):
            return ctx.enter_context(nc.semaphore(name))

        x_full = sb("x_full", [P, TILES * N], F32)
        x_hi = sb("x_hi", [P, TILES * N], F16)
        x_lo = sb("x_lo", [P, TILES * N], F16)
        gx_hi = sb("gx_hi", [P, NE * N], F16)
        gx_lo = sb("gx_lo", [P, NE * N], F16)
        W_COLS = 3 * F
        w_full = sb("w_full", [P, NE * W_COLS], F32)
        w_hi = sb("w_hi", [P, NE * W_COLS], F16)
        w_lo = sb("w_lo", [P, NE * W_COLS], F16)
        gates_in = sb("gates_in", [P, B * (NE - 1)], F32)
        shared_in = sb("shared_in", [P, B], F32)
        rest = sb("rest", [P, B], F32)
        coef = sb("coef", [P, NE * B], F32)
        silu = sb("silu", [P, 2 * N], F32)
        hidden = sb("hidden", [P, 2 * N], F32)
        h_hi = sb("h_hi", [P, CHUNKS * N], F16)
        h_lo = sb("h_lo", [P, CHUNKS * N], F16)
        ident = sb("ident", [P, P], F32)
        ids = sb("ids", [1, B], I32)
        w1_sb = sb("w1_sb", [P, BATCHES * A], F32)
        w2b2_sb = sb("w2b2_sb", [A + 1, BATCHES * D], F32)
        b1_sb = sb("b1_sb", [A, BATCHES], F32)
        affine_sb = sb("affine_sb", [P, B * 2 * D], F32)
        x2T = sb("x2T", [P, N], F32)
        adapt_h = sb("adapt_h", [A + 1, N], F32)
        x2 = sb("x2", [P, N], F32)
        x2_beta = sb("x2_beta", [P, N], F32)
        y = sb("y", [P, N], F32)
        scaled = sb("scaled", [P, N], F32)
        result = sb("result", [P, TILES * N], F32)
        stats = sb("stats", [P, BATCHES * 6], F32)
        mean_sum = sb("mean_sum", [P, BATCHES], F32)
        mean_diff = sb("mean_diff", [P, BATCHES], F32)
        dev_sum = sb("dev_sum", [P, BATCHES], F32)
        between = sb("between", [P, BATCHES], F32)
        mean = sb("mean", [P, BATCHES], F32)
        var_eps = sb("var_eps", [P, BATCHES], F32)
        rstd = sb("rstd", [P, BATCHES], F32)
        minus_half = sb("minus_half", [P, BATCHES], F32)

        gate_ps = [bank("gate_ps0"), bank("gate_ps1")]
        up_ps = [bank("up_ps0"), bank("up_ps1")]
        moe_ps = bank("moe_ps")
        adapt_ps = bank("adapt_ps")
        x2_ps = bank("x2_ps")
        back_ps = bank("back_ps")

        gates_loaded = sem("gates_loaded")
        ids_loaded = sem("ids_loaded")
        x0_loaded = sem("x0_loaded")
        x_rest_loaded = sem("x_rest_loaded")
        w0_loaded = [sem(f"w0_loaded{i}") for i in range(3)]
        w_loaded = [sem(f"w_loaded{e}") for e in range(1, NE)]
        experts_loaded = sem("experts_loaded")
        adapter_loaded = sem("adapter_loaded")
        affine_loaded = sem("affine_loaded")
        stored = sem("stored")
        coef_ready = sem("coef_ready")
        rest_ready = sem("rest_ready")
        x_hi_ready = sem("x_hi_ready")
        x_lo_ready = sem("x_lo_ready")
        w_hi_ready = sem("w_hi_ready")
        w_lo_ready = sem("w_lo_ready")
        gx_hi_ready = sem("gx_hi_ready")
        gx_lo_ready = sem("gx_lo_ready")
        gate_done = sem("gate_done")
        up_done = sem("up_done")
        down_done = sem("down_done")
        silu_ready = sem("silu_ready")
        hidden_ready = sem("hidden_ready")
        h_hi_ready = sem("h_hi_ready")
        h_lo_ready = sem("h_lo_ready")
        ident_zeroed = sem("ident_zeroed")
        consts_ready = sem("consts_ready")
        ones_ready = sem("ones_ready")
        x2T_ready = sem("x2T_ready")
        adapt_done = sem("adapt_done")
        x2_transposed = sem("x2_transposed")
        adapt_h_ready = sem("adapt_h_ready")
        x2_ready = sem("x2_ready")
        back_done = sem("back_done")
        y_ready = sem("y_ready")
        stats_ready = sem("stats_ready")
        halves_ready = sem("halves_ready")
        between_ready = sem("between_ready")
        mean_ready = sem("mean_ready")
        var_eps_ready = sem("var_eps_ready")
        rstd_ready = sem("rstd_ready")
        x2_beta_ready = sem("x2_beta_ready")
        scaled_ready = sem("scaled_ready")
        result_ready = sem("result_ready")

        def cols(tensor, index, width, rows=P):
            return tensor[0:rows, bass.ds(index * width, width)]

        def expert_w(tensor, e, third, f):
            return tensor[:, bass.ds(e * W_COLS + (third * F + f * P), P)]

        block = ctx.enter_context(nc.Block())

        @block.sync
        def _(sp):
            sp.dma_start(x_full[:, 0:N], xT[0]).then_inc(x0_loaded, 16)
            for third in range(3):
                part = slice(third * F, (third + 1) * F)
                sp.dma_start(w_full[:, part], weights[0, :, part]).then_inc(w0_loaded[third], 16)
            for e in range(1, NE):
                sp.dma_start(cols(w_full, e, W_COLS), weights[e]).then_inc(w_loaded[e - 1], 16)
                if e == 1:
                    sp.dma_start(x_full[:, N:].rearrange("p (t n) -> p t n", n=N),
                                 xT[1:].rearrange("t p n -> p t n")).then_inc(x_rest_loaded, 16)
            for e in range(1, NE):
                sp.wait_ge(w_loaded[e - 1], 16)
                sp.sem_inc(experts_loaded, 1)
            sp.wait_ge(ids_loaded, 16)

            def load_adapter(t):
                for q in range(BATCHES):
                    lang = sp.value_load(ids[0:1, bass.ds(t * BATCHES + q, 1)], min_val=0, max_val=LANGS - 1)
                    one = bass.ds(lang, 1)
                    sp.dma_start(w1_sb[:, q * A:(q + 1) * A],
                                 w1[one].rearrange("l h a -> (l h) a")).then_inc(adapter_loaded, 16)
                    sp.dma_start(w2b2_sb[:, q * D:(q + 1) * D],
                                 w2b2[one].rearrange("l a h -> (l a) h")).then_inc(adapter_loaded, 16)
                    sp.dma_start(b1_sb[:, q:q + 1],
                                 b1[one].rearrange("l a o -> (l a) o")).then_inc(adapter_loaded, 16)

            load_adapter(0)
            with sp.Fori(0, B) as b:
                lang = sp.value_load(ids[0:1, bass.ds(b, 1)], min_val=0, max_val=LANGS - 1)
                sp.dma_start(cols(affine_sb, b, 2 * D),
                             affine[bass.ds(lang, 1)].to_broadcast([P, 2 * D])).then_inc(affine_loaded, 16)
            with sp.Fori(0, TILES - 1) as t:
                sp.wait_ge(back_done, t + 1)
                load_adapter(t + 1)
                sp.wait_ge(result_ready, BATCHES * (t + 1))
                sp.dma_start(out[bass.ds(t, 1)].rearrange("o s b h -> (o s) (b h)"),
                             cols(result, t, N)).then_inc(stored, 16)
            for q in range(BATCHES):
                sp.wait_ge(result_ready, BATCHES * (TILES - 1) + q + 1)
                sp.dma_start(out[TILES - 1, :, q],
                             cols(result, (TILES - 1) * BATCHES + q, D)).then_inc(stored, 16)
            sp.wait_ge(stored, 16 * (TILES - 1 + BATCHES))

        @block.tensor
        def _(pe):
            def three_passes(psum, w, e, third, f, act_hi, act_lo, start, stop):
                hi, lo = expert_w(w_hi, e, third, f), expert_w(w_lo, e, third, f)
                nc.tensor.matmul(psum, hi, act_hi, start=start, stop=False)
                nc.tensor.matmul(psum, hi, act_lo, start=False, stop=False)
                return nc.tensor.matmul(psum, lo, act_hi, start=False, stop=stop)

            def gate_up(t, e, f, first_tile):
                n = t * PER_TILE + e * CHUNKS + f
                early = first_tile and isinstance(e, int) and e * CHUNKS + f < 2
                if first_tile:
                    pe.wait_ge(w_lo_ready, 3 * e + 1)
                if not early:
                    pe.wait_ge(silu_ready, n - 1)
                three_passes(gate_ps[f % 2][:, :], w_hi, e, 0, f, cols(x_hi, t, N), cols(x_lo, t, N),
                             True, True).then_inc(gate_done, 1)
                if f == 0:
                    pe.wait_ge(gx_lo_ready, n + CHUNKS)
                if first_tile:
                    pe.wait_ge(w_lo_ready, 3 * e + 2)
                if not early:
                    pe.wait_ge(hidden_ready, n - 1)
                three_passes(up_ps[f % 2][:, :], w_hi, e, 1, f, cols(gx_hi, e, N), cols(gx_lo, e, N),
                             True, True).then_inc(up_done, 1)

            def down(t, e, f, start=False, stop=False):
                n = t * PER_TILE + e * CHUNKS + f
                pe.wait_ge(h_lo_ready, n + 1)
                three_passes(moe_ps[:, :], w_hi, e, 2, f, cols(h_hi, f, N), cols(h_lo, f, N),
                             start, stop).then_inc(down_done, 1)

            def adapter_in(t):
                pe.wait_ge(x2T_ready, t + 1)
                pe.wait_ge(adapter_loaded, 16 * 3 * BATCHES * (t + 1))
                for q in range(BATCHES):
                    part = slice(q * S, (q + 1) * S)
                    last = nc.tensor.matmul(adapt_ps[0:A, part], w1_sb[:, q * A:(q + 1) * A], x2T[:, part],
                                            start=True, stop=True)
                last.then_inc(adapt_done, 1)
                for q in range(BATCHES):
                    part = slice(q * S, (q + 1) * S)
                    last = nc.tensor.transpose(x2_ps[:, part], x2T[:, part], ident[:, :])
                last.then_inc(x2_transposed, 1)

            def adapter_back(t):
                pe.wait_ge(adapt_h_ready, t + 1)
                for q in range(BATCHES):
                    part = slice(q * S, (q + 1) * S)
                    last = nc.tensor.matmul(back_ps[:, part], adapt_h[:, part], w2b2_sb[:, q * D:(q + 1) * D],
                                            start=True, stop=True)
                last.then_inc(back_done, 1)

            def tile(t, first_tile):
                for f in range(CHUNKS):
                    gate_up(t, 0, f, first_tile)
                    if f < 2:
                        if not first_tile:
                            down(t - 1, NE - 1, f + 2, stop=(f == 1))
                    else:
                        if f == 2 and not first_tile:
                            pe.wait_ge(x2T_ready, t)
                        down(t, 0, f - 2, start=(f == 2))
                        if f == 2 and not first_tile:
                            adapter_in(t - 1)
                if not first_tile:
                    adapter_back(t - 1)
                with pe.Fori(1, NE) as e:
                    for f in range(CHUNKS):
                        gate_up(t, e, f, first_tile)
                        if f < 2:
                            down(t, e - 1, f + 2)
                        else:
                            down(t, e, f - 2)

            pe.wait_ge(x_lo_ready, 1)
            tile(0, True)
            pe.wait_ge(x_lo_ready, 2)
            pe.wait_ge(consts_ready, 1)
            with pe.Fori(1, TILES) as t:
                tile(t, False)
            down(TILES - 1, NE - 1, 2)
            down(TILES - 1, NE - 1, 3, stop=True)
            adapter_in(TILES - 1)
            adapter_back(TILES - 1)

        @block.scalar
        def _(act):
            act.dma_start(gates_in[:, :], gates.to_broadcast([P, B * (NE - 1)])).then_inc(gates_loaded, 16)
            act.dma_start(shared_in[:, :], shared_gate.to_broadcast([P, B])).then_inc(gates_loaded, 16)
            act.dma_start(ids[:, :], language).then_inc(ids_loaded, 16)

            def gated_x_hi(t, e, q):
                src = x_full[:, bass.ds(t * N + q * S, S)]
                dst = gx_hi[:, bass.ds(e * N + q * S, S)]
                nc.scalar.activation(dst, src, ACT.Copy,
                                     scale=coef[:, bass.ds(e * B + t * BATCHES + q, 1)]).then_inc(gx_hi_ready, 1)

            def weight_hi(e, third):
                part = bass.ds(e * W_COLS + third * F, F)
                nc.scalar.activation(w_hi[:, part], w_full[:, part], ACT.Copy, scale=W_SCALE).then_inc(w_hi_ready, 1)

            def silu_of(n, f, early):
                act.wait_ge(gate_done, n + 1)
                if not early:
                    act.wait_ge(hidden_ready, n - 1)
                nc.scalar.activation(cols(silu, f % 2, N), gate_ps[f % 2][:, :], ACT.Silu,
                                     scale=1.0 / W_SCALE).then_inc(silu_ready, 1)

            def hidden_hi(n, f, early):
                act.wait_ge(hidden_ready, n + 1)
                if not early:
                    act.wait_ge(down_done, n - 3)
                nc.scalar.activation(cols(h_hi, f, N), cols(hidden, f % 2, N), ACT.Copy).then_inc(h_hi_ready, 1)

            def adapter_relu(t):
                act.wait_ge(adapt_done, t + 1)
                act.wait_ge(adapter_loaded, 16 * 3 * BATCHES * (t + 1))
                for q in range(BATCHES):
                    part = slice(q * S, (q + 1) * S)
                    last = nc.scalar.activation(adapt_h[0:A, part], adapt_ps[0:A, part], ACT.Relu,
                                                bias=b1_sb[:, q:q + 1])
                last.then_inc(adapt_h_ready, 1)
                act.wait_ge(x2_transposed, t + 1)
                nc.scalar.activation(x2[:, :], x2_ps[:, :], ACT.Copy).then_inc(x2_ready, 1)

            def expert(t, e, first_tile, next_w, next_gx, adapter_of=None):
                for f in range(CHUNKS):
                    n = t * PER_TILE + e * CHUNKS + f
                    at_start = first_tile and isinstance(e, int) and e == 0
                    silu_of(n, f, at_start and f < 2)
                    if next_w is not None and f < 3:
                        if f == 0:
                            act.wait_ge(experts_loaded, next_w)
                        weight_hi(next_w, f)
                    if next_gx is not None:
                        gated_x_hi(next_gx[0], next_gx[1], f)
                    hidden_hi(n, f, at_start)
                    if adapter_of is not None and f == 2:
                        adapter_relu(adapter_of)

            act.wait_ge(x0_loaded, 16)
            nc.scalar.activation(x_hi[:, 0:N], x_full[:, 0:N], ACT.Copy).then_inc(x_hi_ready, 1)
            act.wait_ge(w0_loaded[0], 16)
            weight_hi(0, 0)
            act.wait_ge(coef_ready, 1)
            for q in range(BATCHES):
                gated_x_hi(0, 0, q)
            for third in (1, 2):
                act.wait_ge(w0_loaded[third], 16)
                weight_hi(0, third)
            expert(0, 0, True, 1, (0, 1))
            act.wait_ge(x_rest_loaded, 16)
            nc.scalar.activation(x_hi[:, N:], x_full[:, N:], ACT.Copy).then_inc(x_hi_ready, 1)
            with act.Fori(1, NE - 1) as e:
                expert(0, e, True, e + 1, (0, e + 1))
            expert(0, NE - 1, True, None, (1, 0))

            def tile(t, last_tile):
                expert(t, 0, False, None, (t, 1), adapter_of=t - 1)
                with act.Fori(1, NE - 1) as e:
                    expert(t, e, False, None, (t, e + 1))
                expert(t, NE - 1, False, None, None if last_tile else (t + 1, 0))

            with act.Fori(1, TILES - 1) as t:
                tile(t, False)
            tile(TILES - 1, True)
            adapter_relu(TILES - 1)

        @block.vector
        def _(dve):
            def gated_x_lo(t, e, q):
                dve.wait_ge(gx_hi_ready, (t * NE + e) * CHUNKS + q + 1)
                part = bass.ds(e * N + q * S, S)
                nc.vector.scalar_tensor_tensor(out=gx_lo[:, part], in0=x_full[:, bass.ds(t * N + q * S, S)],
                                               scalar=coef[:, bass.ds(e * B + t * BATCHES + q, 1)],
                                               in1=gx_hi[:, part], op0=ALU.mult,
                                               op1=ALU.subtract).then_inc(gx_lo_ready, 1)

            def weight_lo(e, third):
                part = bass.ds(e * W_COLS + third * F, F)
                dve.wait_ge(w_hi_ready, 3 * e + third + 1)
                nc.vector.scalar_tensor_tensor(out=w_lo[:, part], in0=w_full[:, part], scalar=W_SCALE,
                                               in1=w_hi[:, part], op0=ALU.mult,
                                               op1=ALU.subtract).then_inc(w_lo_ready, 1)

            def hidden_of(n, f, early):
                dve.wait_ge(silu_ready, n + 1)
                if not early:
                    dve.wait_ge(h_hi_ready, n - 1)
                dve.wait_ge(up_done, n + 1)
                nc.vector.scalar_tensor_tensor(out=cols(hidden, f % 2, N), in0=cols(silu, f % 2, N),
                                               scalar=HIDDEN_RESCALE, in1=up_ps[f % 2][:, :], op0=ALU.mult,
                                               op1=ALU.mult).then_inc(hidden_ready, 1)

            def hidden_lo(n, f):
                dve.wait_ge(h_hi_ready, n + 1)
                nc.vector.tensor_tensor(cols(h_lo, f, N), cols(hidden, f % 2, N), cols(h_hi, f, N),
                                        ALU.subtract).then_inc(h_lo_ready, 1)

            def moe_out(t):
                dve.wait_ge(down_done, PER_TILE * (t + 1))
                nc.vector.scalar_tensor_tensor(out=x2T[:, :], in0=moe_ps[:, :], scalar=OUT_RESCALE,
                                               in1=cols(x_full, t, N), op0=ALU.mult,
                                               op1=ALU.add).then_inc(x2T_ready, 1)

            def norm_stats(t, q):
                done = t * BATCHES + q + 1
                if isinstance(q, int) and q == 0 or not isinstance(q, int):
                    dve.wait_ge(back_done, t + 1)
                    dve.wait_ge(x2_ready, t + 1)
                nc.vector.tensor_tensor(cols(y, q, D), cols(back_ps, q, D), cols(x2, q, D),
                                        ALU.add).then_inc(y_ready, 1)
                dve.wait_ge(y_ready, done)
                nc.vector.bn_stats(cols(stats, q, 6), cols(y, q, D)).then_inc(stats_ready, 1)

            def norm_moments(t):
                half = stats[:, :].rearrange("p (q s) -> p q s", s=6)
                mean_even, dev_even, mean_odd, dev_odd = half[:, :, 1], half[:, :, 2], half[:, :, 4], half[:, :, 5]
                dve.wait_ge(stats_ready, BATCHES * (t + 1))
                nc.vector.tensor_tensor(mean_sum[:, :], mean_even, mean_odd, ALU.add).then_inc(halves_ready, 1)
                nc.vector.tensor_tensor(mean_diff[:, :], mean_even, mean_odd, ALU.subtract).then_inc(halves_ready, 1)
                nc.vector.scalar_tensor_tensor(out=dev_sum[:, :], in0=dev_even, scalar=D * LN_EPS, in1=dev_odd,
                                               op0=ALU.add, op1=ALU.add).then_inc(halves_ready, 1)
                dve.wait_ge(halves_ready, 3 * (t + 1))
                nc.vector.tensor_scalar(mean[:, :], mean_sum[:, :], 0.5, None, ALU.mult).then_inc(mean_ready, 1)
                nc.vector.scalar_tensor_tensor(out=between[:, :], in0=mean_diff[:, :], scalar=0.25,
                                               in1=mean_diff[:, :], op0=ALU.mult,
                                               op1=ALU.mult).then_inc(between_ready, 1)
                dve.wait_ge(between_ready, t + 1)
                nc.vector.scalar_tensor_tensor(out=var_eps[:, :], in0=dev_sum[:, :], scalar=1.0 / D,
                                               in1=between[:, :], op0=ALU.mult,
                                               op1=ALU.add).then_inc(var_eps_ready, 1)

            def norm_out(t, q):
                dve.wait_ge(affine_loaded, 16 * B)
                dve.wait_ge(mean_ready, t + 1)
                gamma = affine_sb[:, bass.ds((t * BATCHES + q) * 2 * D, D)]
                nc.vector.scalar_tensor_tensor(out=cols(scaled, q, D), in0=cols(y, q, D),
                                               scalar=mean[:, bass.ds(q, 1)], in1=gamma,
                                               op0=ALU.subtract, op1=ALU.mult).then_inc(scaled_ready, 1)
                dve.wait_ge(x2_beta_ready, t + 1)
                dve.wait_ge(rstd_ready, t + 1)
                dve.wait_ge(scaled_ready, t * BATCHES + q + 1)
                nc.vector.scalar_tensor_tensor(out=cols(result, t * BATCHES + q, D), in0=cols(scaled, q, D),
                                               scalar=rstd[:, bass.ds(q, 1)], in1=cols(x2_beta, q, D),
                                               op0=ALU.mult, op1=ALU.add).then_inc(result_ready, 1)

            def expert(t, e, first_tile, next_w, next_gx, evacuate=None, extra=None):
                for f in range(CHUNKS):
                    n = t * PER_TILE + e * CHUNKS + f
                    at_start = first_tile and isinstance(e, int) and e == 0
                    hidden_of(n, f, at_start and f < 2)
                    if next_w is not None and f < 3:
                        weight_lo(next_w, f)
                    if next_gx is not None:
                        gated_x_lo(next_gx[0], next_gx[1], f)
                    if evacuate is not None and f == 1:
                        moe_out(evacuate)
                    hidden_lo(n, f)
                    if extra is not None and f == 1:
                        extra()

            nc.vector.memset(adapt_h[A:A + 1, :], 1.0).then_inc(ones_ready, 1)
            dve.wait_ge(gates_loaded, 32)
            nc.vector.tensor_scalar(rest[:, :], shared_in[:, :], -X_SCALE, X_SCALE, ALU.mult,
                                    ALU.add).then_inc(rest_ready, 1)
            nc.vector.tensor_scalar(coef[:, (NE - 1) * B:], shared_in[:, :], X_SCALE, None, ALU.mult)
            dve.wait_ge(rest_ready, 1)
            per_expert = coef[:, 0:(NE - 1) * B].rearrange("p (e b) -> p e b", b=B)
            nc.vector.tensor_tensor(per_expert, gates_in[:, :].rearrange("p (b e) -> p e b", b=B),
                                    rest[:, :].rearrange("p (o b) -> p o b", o=1).to_broadcast([P, NE - 1, B]),
                                    ALU.mult).then_inc(coef_ready, 1)
            dve.wait_ge(x_hi_ready, 1)
            nc.vector.tensor_tensor(x_lo[:, 0:N], x_full[:, 0:N], x_hi[:, 0:N],
                                    ALU.subtract).then_inc(x_lo_ready, 1)
            weight_lo(0, 0)
            dve.wait_ge(coef_ready, 1)
            for q in range(BATCHES):
                gated_x_lo(0, 0, q)
            weight_lo(0, 1)
            weight_lo(0, 2)
            expert(0, 0, True, 1, (0, 1))
            dve.wait_ge(x_hi_ready, 2)
            nc.vector.tensor_tensor(x_lo[:, N:], x_full[:, N:], x_hi[:, N:], ALU.subtract).then_inc(x_lo_ready, 1)
            with dve.Fori(1, NE - 1) as e:
                expert(0, e, True, e + 1, (0, e + 1))
            expert(0, NE - 1, True, None, (1, 0))

            def tile(t, last_tile):
                expert(t, 0, False, None, (t, 1), evacuate=t - 1)
                with dve.Fori(1, 1 + BATCHES) as e:
                    expert(t, e, False, None, (t, e + 1), extra=lambda: norm_stats(t - 1, e - 1))
                norm_moments(t - 1)
                with dve.Fori(1 + BATCHES, NE - 1) as e:
                    expert(t, e, False, None, (t, e + 1),
                           extra=lambda: norm_out(t - 1, e - 1 - BATCHES))
                expert(t, NE - 1, False, None, None if last_tile else (t + 1, 0),
                       extra=lambda: norm_out(t - 1, BATCHES - 1))

            with dve.Fori(1, TILES - 1) as t:
                tile(t, False)
            tile(TILES - 1, True)
            moe_out(TILES - 1)
            for q in range(BATCHES):
                norm_stats(TILES - 1, q)
            norm_moments(TILES - 1)
            for q in range(BATCHES):
                norm_out(TILES - 1, q)

        @block.gpsimd
        def _(pool):
            nc.gpsimd.memset(ident[:, :], 0.0).then_inc(ident_zeroed, 1)
            nc.gpsimd.memset(minus_half[:, :], -0.5).then_inc(ident_zeroed, 1)
            pool.wait_ge(ident_zeroed, 2)
            nc.gpsimd.affine_select(out=ident[:, :], in_=ident[:, :], compare_op=ALU.not_equal, fill=1.0, base=0,
                                    pattern=[[-1, P]], channel_multiplier=1).then_inc(consts_ready, 1)
            affine_v = affine_sb[:, :].rearrange("p (q two h) -> p q two h", two=2, h=D)
            x2_v = x2[:, :].rearrange("p (q h) -> p q h", h=D)
            x2_beta_v = x2_beta[:, :].rearrange("p (q h) -> p q h", h=D)
            pool.wait_ge(affine_loaded, 16 * B)
            for t in range(TILES):
                pool.wait_ge(x2_ready, t + 1)
                beta = affine_v[:, t * BATCHES:(t + 1) * BATCHES, 1]
                nc.gpsimd.tensor_tensor(x2_beta_v, x2_v, beta, ALU.add).then_inc(x2_beta_ready, 1)
                pool.wait_ge(var_eps_ready, t + 1)
                nc.gpsimd.tensor_tensor(rstd[:, :], var_eps[:, :], minus_half[:, :], ALU.pow).then_inc(rstd_ready, 1)


_OUT = "out_dram"


def kernel(**inputs):
    import numpy as np
    import concourse.bacc as bacc
    from concourse.bass_utils import run_bass_kernel_spmd

    a = {name: np.asarray(value) for name, value in inputs.items()}
    wg = np.concatenate([a["L0_cond_Wg"], a["L0_cond_Sg"][None]])
    wu = np.concatenate([a["L0_cond_Wu"], a["L0_cond_Su"][None]])
    wd = np.concatenate([a["L0_cond_Wd"], a["L0_cond_Sd"][None]])
    wd = wd.reshape(NE, CHUNKS, P, D).transpose(0, 2, 1, 3).reshape(NE, P, F)
    arrays = {
        "xT": a["x"].reshape(TILES, N, D).transpose(0, 2, 1),
        "weights": np.concatenate([wg, wu, wd], axis=2),
        "gates": a["fside_Bx8_0"].reshape(1, B * (NE - 1)),
        "shared_gate": a["condB_sharedgateprob"].reshape(1, B),
        "language": a["itok_B_0_8"].reshape(1, B),
        "w1": a["L1_cond_W1"],
        "w2b2": np.concatenate([a["L1_cond_W2"], a["L1_cond_b2"][:, None]], axis=1),
        "b1": a["L1_cond_b1"][:, :, None],
        "affine": np.concatenate([a["L1_cond_gamma"], a["L1_cond_beta"]], axis=1),
    }
    nc = bacc.Bacc("TRN2", target_bir_lowering=False, num_devices=1)
    args = []
    for name in list(arrays):
        arrays[name] = np.ascontiguousarray(arrays[name])
        args.append(nc.dram_tensor(name, arrays[name].shape, mybir.dt.from_np(arrays[name].dtype),
                                   kind="ExternalInput").ap())
    out = nc.dram_tensor(_OUT, (TILES, S, BATCHES, D), F32, kind="ExternalOutput").ap()
    build(nc, *args, out)
    done = run_bass_kernel_spmd(nc, [arrays], core_ids=[0])
    return done.results[0][_OUT].transpose(0, 2, 1, 3).reshape(B, S, D)
```

```python
from contextlib import ExitStack

import concourse.bass as bass
from concourse import mybir

P = 128
B, S, D = 16, 128, 128
NE, F = 9, 512
CHUNKS = F // P
TILES = 4
BATCHES = B // TILES
N = BATCHES * S
PER_TILE = NE * CHUNKS
A = 32
LANGS = 10
LAG = 3
LN_EPS = 1e-5
WARM_UP = 9
GATED_AT = [(0, 1), (2,), (3,), ()]

W_SCALE = 64.0
X_SCALE = 8.0
H_SCALE = 32.0
HIDDEN_RESCALE = H_SCALE / (W_SCALE * X_SCALE)
OUT_RESCALE = 1.0 / (W_SCALE * H_SCALE)

F32 = mybir.dt.float32
F16 = mybir.dt.float16
I32 = mybir.dt.int32
ALU = mybir.AluOpType
ACT = mybir.ActivationFunctionType


def build(nc, xT, weights, gates, language, w1, w2b2, b1, affine, out):
    with ExitStack() as ctx:
        def sb(name, shape, dt):
            return ctx.enter_context(nc.sbuf_tensor(name, shape, dt))

        def bank(name):
            return ctx.enter_context(nc.psum_tensor(name, [P, N], F32))

        def sem(name):
            return ctx.enter_context(nc.semaphore(name))

        x_full = sb("x_full", [P, TILES * N], F32)
        x_hi = sb("x_hi", [P, TILES * N], F16)
        x_lo = sb("x_lo", [P, TILES * N], F16)
        gx_hi = sb("gx_hi", [P, NE * N], F16)
        gx_lo = sb("gx_lo", [P, NE * N], F16)
        W_COLS = 3 * F
        w_full = sb("w_full", [P, NE * W_COLS], F32)
        w_hi = sb("w_hi", [P, NE * W_COLS], F16)
        w_lo = sb("w_lo", [P, NE * W_COLS], F16)
        down64 = sb("down64", [P, F], F32)
        w_scale = sb("w_scale", [P, F], F32)
        warm = sb("warm", [P, F], F16)
        gates_in = sb("gates_in", [P, B * NE], F32)
        rest = sb("rest", [P, B], F32)
        coef = sb("coef", [P, NE * B], F32)
        silu = sb("silu", [P, 2 * N], F32)
        hidden = sb("hidden", [P, 2 * N], F32)
        h_hi = sb("h_hi", [P, CHUNKS * N], F16)
        h_lo = sb("h_lo", [P, CHUNKS * N], F16)
        ident = sb("ident", [P, P], F32)
        ids = sb("ids", [1, B], I32)
        w1_sb = sb("w1_sb", [P, BATCHES * A], F32)
        w2b2_sb = sb("w2b2_sb", [A + 1, BATCHES * D], F32)
        b1_sb = sb("b1_sb", [A, BATCHES], F32)
        affine_sb = sb("affine_sb", [P, B * 2 * D], F32)
        x2T = sb("x2T", [P, N], F32)
        adapt_h = sb("adapt_h", [A + 1, N], F32)
        x2 = sb("x2", [P, N], F32)
        x2_beta = sb("x2_beta", [P, N], F32)
        y = sb("y", [P, N], F32)
        scaled = sb("scaled", [P, N], F32)
        result = sb("result", [P, TILES * N], F32)
        stats = sb("stats", [P, BATCHES * 6], F32)
        mean_sum = sb("mean_sum", [P, BATCHES], F32)
        mean_diff = sb("mean_diff", [P, BATCHES], F32)
        dev_sum = sb("dev_sum", [P, BATCHES], F32)
        between = sb("between", [P, BATCHES], F32)
        mean = sb("mean", [P, BATCHES], F32)
        var_eps = sb("var_eps", [P, BATCHES], F32)
        rstd = sb("rstd", [P, BATCHES], F32)
        minus_half = sb("minus_half", [P, BATCHES], F32)

        gate_ps = [bank("gate_ps0"), bank("gate_ps1")]
        up_ps = [bank("up_ps0"), bank("up_ps1")]
        moe_ps = bank("moe_ps")
        adapt_ps = bank("adapt_ps")
        x2_ps = bank("x2_ps")
        back_ps = bank("back_ps")
        tail_in_ps = [adapt_ps, back_ps, x2_ps, moe_ps]
        tail_y_ps = gate_ps + up_ps

        gates_loaded = sem("gates_loaded")
        ids_loaded = sem("ids_loaded")
        x0_loaded = sem("x0_loaded")
        x_rest_loaded = sem("x_rest_loaded")
        x_rest_hi_ready = sem("x_rest_hi_ready")
        x_rest_ready = sem("x_rest_ready")
        warm_ready = sem("warm_ready")
        w_scale_ready = sem("w_scale_ready")
        down64_ready = sem("down64_ready")
        down_hi_ready = sem("down_hi_ready")
        w_down_ready = sem("w_down_ready")
        w0_loaded = [sem(f"w0_loaded{i}") for i in range(3)]
        w_loaded = [sem(f"w_loaded{e}") for e in range(1, NE)]
        experts_loaded = sem("experts_loaded")
        adapter_loaded = sem("adapter_loaded")
        affine_loaded = sem("affine_loaded")
        stored = sem("stored")
        coef_ready = sem("coef_ready")
        rest_ready = sem("rest_ready")
        x_hi_ready = sem("x_hi_ready")
        x_lo_ready = sem("x_lo_ready")
        w_hi_ready = sem("w_hi_ready")
        w_lo_ready = sem("w_lo_ready")
        gx_hi_ready = sem("gx_hi_ready")
        gx_lo_ready = sem("gx_lo_ready")
        gate_done = sem("gate_done")
        up_done = sem("up_done")
        down_done = sem("down_done")
        silu_ready = sem("silu_ready")
        hidden_ready = sem("hidden_ready")
        h_hi_ready = sem("h_hi_ready")
        h_lo_ready = sem("h_lo_ready")
        ident_zeroed = sem("ident_zeroed")
        consts_ready = sem("consts_ready")
        ones_ready = sem("ones_ready")
        x2T_ready = sem("x2T_ready")
        adapt_done = sem("adapt_done")
        x2_transposed = sem("x2_transposed")
        adapt_h_ready = sem("adapt_h_ready")
        x2_ready = sem("x2_ready")
        back_done = sem("back_done")
        y_ready = sem("y_ready")
        stats_ready = sem("stats_ready")
        halves_ready = sem("halves_ready")
        between_ready = sem("between_ready")
        mean_ready = sem("mean_ready")
        var_eps_ready = sem("var_eps_ready")
        rstd_ready = sem("rstd_ready")
        x2_beta_ready = sem("x2_beta_ready")
        scaled_ready = sem("scaled_ready")
        result_ready = sem("result_ready")

        def cols(tensor, index, width, rows=P):
            return tensor[0:rows, bass.ds(index * width, width)]

        def expert_w(tensor, e, third, f):
            return tensor[:, bass.ds(e * W_COLS + (third * F + f * P), P)]

        block = ctx.enter_context(nc.Block())

        @block.sync
        def _(sp):
            sp.dma_start(x_full[:, 0:N], xT[0]).then_inc(x0_loaded, 16)
            for third in range(3):
                part = slice(third * F, (third + 1) * F)
                sp.dma_start(w_full[:, part], weights[0, :, part]).then_inc(w0_loaded[third], 16)
            for e in range(1, NE):
                sp.dma_start(cols(w_full, e, W_COLS), weights[e]).then_inc(w_loaded[e - 1], 16)
                if e == 1:
                    sp.dma_start(x_full[:, N:].rearrange("p (t n) -> p t n", n=N),
                                 xT[1:].rearrange("t p n -> p t n")).then_inc(x_rest_loaded, 16)
            for e in range(1, NE):
                sp.wait_ge(w_loaded[e - 1], 16)
                sp.sem_inc(experts_loaded, 1)
            sp.wait_ge(ids_loaded, 16)

            def load_adapter(t):
                for q in range(BATCHES):
                    lang = sp.value_load(ids[0:1, bass.ds(t * BATCHES + q, 1)], min_val=0, max_val=LANGS - 1)
                    one = bass.ds(lang, 1)
                    sp.dma_start(w1_sb[:, q * A:(q + 1) * A],
                                 w1[one].rearrange("l h a -> (l h) a")).then_inc(adapter_loaded, 16)
                    sp.dma_start(w2b2_sb[:, q * D:(q + 1) * D],
                                 w2b2[one].rearrange("l a h -> (l a) h")).then_inc(adapter_loaded, 16)
                    sp.dma_start(b1_sb[:, q:q + 1],
                                 b1[one].rearrange("l a o -> (l a) o")).then_inc(adapter_loaded, 16)

            load_adapter(0)
            with sp.Fori(0, B) as b:
                lang = sp.value_load(ids[0:1, bass.ds(b, 1)], min_val=0, max_val=LANGS - 1)
                sp.dma_start(cols(affine_sb, b, 2 * D),
                             affine[bass.ds(lang, 1)].to_broadcast([P, 2 * D])).then_inc(affine_loaded, 16)
            with sp.Fori(0, TILES - 1) as t:
                sp.wait_ge(back_done, t + 1)
                load_adapter(t + 1)
                sp.wait_ge(result_ready, BATCHES * (t + 1))
                sp.dma_start(out[bass.ds(t, 1)].rearrange("o s b h -> (o s) (b h)"),
                             cols(result, t, N)).then_inc(stored, 16)
            sp.wait_ge(result_ready, BATCHES * (TILES - 1) + BATCHES // 2)
            sp.dma_start(out[TILES - 1, :, 0:BATCHES // 2].rearrange("s b h -> s (b h)"),
                         cols(result, 2 * (TILES - 1), N // 2)).then_inc(stored, 16)
            sp.wait_ge(stored, 16 * (TILES - 1 + 2))

        @block.tensor
        def _(pe):
            def three_passes(psum, e, third, f, act_hi, act_lo):
                hi, lo = expert_w(w_hi, e, third, f), expert_w(w_lo, e, third, f)
                nc.tensor.matmul(psum, hi, act_hi, start=True, stop=False)
                nc.tensor.matmul(psum, hi, act_lo, start=False, stop=False)
                return nc.tensor.matmul(psum, lo, act_hi, start=False, stop=True)

            def gate_up(t, e, f, first_tile):
                n = t * PER_TILE + e * CHUNKS + f
                if first_tile:
                    pe.wait_ge(w_lo_ready, 2 * e + 1)
                pe.wait_ge(silu_ready, n - 1)
                three_passes(gate_ps[f % 2][:, :], e, 0, f, cols(x_hi, t, N), cols(x_lo, t, N)).then_inc(gate_done, 1)
                if f == 0:
                    pe.wait_ge(gx_lo_ready, n + CHUNKS)
                if first_tile:
                    pe.wait_ge(w_lo_ready, 2 * e + 2)
                pe.wait_ge(hidden_ready, n - 1)
                three_passes(up_ps[f % 2][:, :], e, 1, f, cols(gx_hi, e, N), cols(gx_lo, e, N)).then_inc(up_done, 1)

            def first_gates_ups():
                def passes(psum, third, f, act_hi, act_lo, act_hi_sem, act_lo_sem, parts):
                    hi, lo = expert_w(w_hi, 0, third, f), expert_w(w_lo, 0, third, f)
                    pe.wait_ge(act_hi_sem, parts)
                    pe.wait_ge(w_hi_ready, third + 1)
                    nc.tensor.matmul(psum, hi, act_hi[:, 0:N], start=True, stop=False)
                    pe.wait_ge(act_lo_sem, parts)
                    nc.tensor.matmul(psum, hi, act_lo[:, 0:N], start=False, stop=False)
                    pe.wait_ge(w_lo_ready, third + 1)
                    return nc.tensor.matmul(psum, lo, act_hi[:, 0:N], start=False, stop=True)

                for f in range(2):
                    passes(gate_ps[f][:, :], 0, f, x_hi, x_lo, x_hi_ready, x_lo_ready, 1).then_inc(gate_done, 1)
                for f in range(2):
                    passes(up_ps[f][:, :], 1, f, gx_hi, gx_lo, gx_hi_ready, gx_lo_ready,
                           BATCHES).then_inc(up_done, 1)

            def down(t, e, f, first_tile=False, start=False, stop=False):
                n = t * PER_TILE + e * CHUNKS + f
                if first_tile and f == 0:
                    pe.wait_ge(w_down_ready, e + 1)
                hi, lo = expert_w(w_hi, e, 2, f), expert_w(w_lo, e, 2, f)
                pe.wait_ge(h_hi_ready, n + 1)
                nc.tensor.matmul(moe_ps[:, :], hi, cols(h_hi, f, N), start=start, stop=False)
                nc.tensor.matmul(moe_ps[:, :], lo, cols(h_hi, f, N), start=False, stop=False)
                pe.wait_ge(h_lo_ready, n + 1)
                nc.tensor.matmul(moe_ps[:, :], hi, cols(h_lo, f, N), start=False, stop=stop).then_inc(down_done, 1)

            def adapter_in(t):
                pe.wait_ge(x2T_ready, t + 1)
                pe.wait_ge(adapter_loaded, 16 * 3 * BATCHES * (t + 1))
                for q in range(BATCHES):
                    part = slice(q * S, (q + 1) * S)
                    last = nc.tensor.matmul(adapt_ps[0:A, part], w1_sb[:, q * A:(q + 1) * A], x2T[:, part],
                                            start=True, stop=True)
                last.then_inc(adapt_done, 1)
                transpose_x2()

            def transpose_x2():
                for q in range(BATCHES):
                    part = slice(q * S, (q + 1) * S)
                    last = nc.tensor.transpose(x2_ps[:, part], x2T[:, part], ident[:, :])
                last.then_inc(x2_transposed, 1)

            def adapter_back(t):
                pe.wait_ge(adapt_h_ready, BATCHES * (t + 1))
                for q in range(BATCHES):
                    part = slice(q * S, (q + 1) * S)
                    last = nc.tensor.matmul(back_ps[:, part], adapt_h[:, part], w2b2_sb[:, q * D:(q + 1) * D],
                                            start=True, stop=True)
                last.then_inc(back_done, 1)

            def expert(t, e, first_tile, middle=None):
                for f in range(CHUNKS):
                    gate_up(t, e, f, first_tile)
                    if f < LAG:
                        down(t, e - 1, CHUNKS - LAG + f)
                    else:
                        down(t, e, f - LAG, first_tile)
                    if middle is not None and f == 0:
                        middle()

            def first_expert(t, first_tile):
                for f in range(CHUNKS):
                    if not (first_tile and f < 2):
                        gate_up(t, 0, f, first_tile)
                    if f < LAG:
                        if not first_tile:
                            down(t - 1, NE - 1, CHUNKS - LAG + f, stop=(f == LAG - 1))
                    else:
                        if f == LAG and not first_tile:
                            pe.wait_ge(x2T_ready, t)
                        down(t, 0, f - LAG, first_tile, start=(f == LAG))
                if not first_tile:
                    adapter_in(t - 1)

            pe.wait_ge(warm_ready, 1)
            for _ in range(WARM_UP):
                nc.tensor.matmul(moe_ps[:, :], warm[:, 0:P], warm[:, :], start=True, stop=True)
            first_gates_ups()
            first_expert(0, True)
            with pe.Fori(1, NE) as e:
                expert(0, e, True)
            pe.wait_ge(x_rest_ready, TILES - 1)
            pe.wait_ge(consts_ready, 1)
            with pe.Fori(1, TILES) as t:
                first_expert(t, False)
                expert(t, 1, False, middle=lambda: adapter_back(t - 1))
                with pe.Fori(2, NE) as e:
                    expert(t, e, False)
            for f in range(CHUNKS - LAG, CHUNKS):
                down(TILES - 1, NE - 1, f, stop=(f == CHUNKS - 1))
            last_tile = TILES - 1
            pe.wait_ge(adapter_loaded, 16 * 3 * BATCHES * TILES)
            for q in range(BATCHES):
                part = slice(q * S, (q + 1) * S)
                pe.wait_ge(x2T_ready, last_tile + q + 1)
                nc.tensor.matmul(tail_in_ps[q][0:A, 0:S], w1_sb[:, q * A:(q + 1) * A], x2T[:, part],
                                 start=True, stop=True).then_inc(adapt_done, 1)
            for q in range(BATCHES):
                part = slice(q * S, (q + 1) * S)
                nc.tensor.matmul(tail_y_ps[q][:, 0:D], x2T[:, part], ident[:, :], start=True, stop=False,
                                 is_transpose=True)
                pe.wait_ge(adapt_h_ready, BATCHES * last_tile + q + 1)
                nc.tensor.matmul(tail_y_ps[q][:, 0:D], adapt_h[:, part], w2b2_sb[:, q * D:(q + 1) * D],
                                 start=False, stop=True).then_inc(back_done, 1)
            pe.wait_ge(affine_loaded, 16 * B)
            for q in range(BATCHES):
                part = slice(q * S, (q + 1) * S)
                beta = slice((last_tile * BATCHES + q) * 2 * D + D, (last_tile * BATCHES + q + 1) * 2 * D)
                nc.tensor.matmul(x2_ps[:, part], x2T[:, part], ident[:, :], start=True, stop=False,
                                 is_transpose=True)
                last = nc.tensor.matmul(x2_ps[:, part], adapt_h[A:A + 1, part], affine_sb[A:A + 1, beta],
                                        start=False, stop=True)
            last.then_inc(x2_transposed, 1)

        @block.scalar
        def _(act):
            nc.scalar.preload_act_table(ACT.Silu)
            act.dma_start(gates_in[:, :], gates.to_broadcast([P, B * NE])).then_inc(gates_loaded, 16)
            act.dma_start(ids[:, :], language).then_inc(ids_loaded, 16)

            def gated_x_hi(t, e, q):
                src = x_full[:, bass.ds(t * N + q * S, S)]
                dst = gx_hi[:, bass.ds(e * N + q * S, S)]
                nc.scalar.activation(dst, src, ACT.Copy,
                                     scale=coef[:, bass.ds(e * B + t * BATCHES + q, 1)]).then_inc(gx_hi_ready, 1)

            def weight_hi(e, third):
                part = bass.ds(e * W_COLS + third * F, F)
                nc.scalar.activation(w_hi[:, part], w_full[:, part], ACT.Copy, scale=W_SCALE).then_inc(w_hi_ready, 1)

            def silu_of(n, f, early):
                act.wait_ge(gate_done, n + 1)
                if not early:
                    act.wait_ge(hidden_ready, n - 1)
                nc.scalar.activation(cols(silu, f % 2, N), gate_ps[f % 2][:, :], ACT.Silu,
                                     scale=1.0 / W_SCALE).then_inc(silu_ready, 1)

            def hidden_hi(n, f):
                act.wait_ge(hidden_ready, n + 1)
                nc.scalar.activation(cols(h_hi, f, N), cols(hidden, f % 2, N), ACT.Copy).then_inc(h_hi_ready, 1)

            def adapter_relu(t):
                act.wait_ge(adapt_done, t + 1)
                act.wait_ge(adapter_loaded, 16 * 3 * BATCHES * (t + 1))
                for q in range(BATCHES):
                    part = slice(q * S, (q + 1) * S)
                    nc.scalar.activation(adapt_h[0:A, part], adapt_ps[0:A, part], ACT.Relu,
                                         bias=b1_sb[:, q:q + 1]).then_inc(adapt_h_ready, 1)
                act.wait_ge(x2_transposed, t + 1)
                nc.scalar.activation(x2[:, :], x2_ps[:, :], ACT.Copy).then_inc(x2_ready, 1)

            def expert(t, e, first_tile, next_w, next_gx, adapter_of=None):
                for f in range(CHUNKS):
                    n = t * PER_TILE + e * CHUNKS + f
                    at_start = first_tile and isinstance(e, int) and e == 0
                    silu_of(n, f, at_start and f < 2)
                    if not (at_start and f == 0):
                        hidden_hi(n - 1, (f - 1) % CHUNKS)
                    if at_start and f == 0:
                        for q in range(BATCHES):
                            gated_x_hi(0, 1, q)
                    if next_w is not None and f < 2:
                        if f == 0:
                            act.wait_ge(experts_loaded, next_w)
                        weight_hi(next_w, f)
                    if next_gx is not None:
                        for q in GATED_AT[f]:
                            gated_x_hi(next_gx[0], next_gx[1], q)
                    if adapter_of is not None and f == CHUNKS - 1:
                        adapter_relu(adapter_of)

            act.wait_ge(x0_loaded, 16)
            nc.scalar.activation(x_hi[:, 0:N], x_full[:, 0:N], ACT.Copy).then_inc(x_hi_ready, 1)
            act.wait_ge(w0_loaded[0], 16)
            weight_hi(0, 0)
            act.wait_ge(coef_ready, 1)
            for q in range(BATCHES):
                gated_x_hi(0, 0, q)
            act.wait_ge(w0_loaded[1], 16)
            weight_hi(0, 1)
            expert(0, 0, True, 1, None)
            with act.Fori(1, NE - 1) as e:
                expert(0, e, True, e + 1, (0, e + 1))
            expert(0, NE - 1, True, None, (1, 0))

            def tile(t, last_tile):
                expert(t, 0, False, None, (t, 1), adapter_of=t - 1)
                with act.Fori(1, NE - 1) as e:
                    expert(t, e, False, None, (t, e + 1))
                expert(t, NE - 1, False, None, None if last_tile else (t + 1, 0))

            with act.Fori(1, TILES - 1) as t:
                tile(t, False)
            tile(TILES - 1, True)
            hidden_hi(TILES * PER_TILE - 1, CHUNKS - 1)
            for q in range(BATCHES):
                part = slice(q * S, (q + 1) * S)
                act.wait_ge(adapt_done, TILES - 1 + q + 1)
                nc.scalar.activation(adapt_h[0:A, part], tail_in_ps[q][0:A, 0:S], ACT.Relu,
                                     bias=b1_sb[:, q:q + 1]).then_inc(adapt_h_ready, 1)
            act.wait_ge(result_ready, BATCHES * TILES)
            act.dma_start(out[TILES - 1, :, BATCHES // 2:].rearrange("s b h -> s (b h)"),
                          cols(result, 2 * TILES - 1, N // 2)).then_inc(stored, 16)

        @block.vector
        def _(dve):
            def gated_x_lo(t, e, q):
                dve.wait_ge(gx_hi_ready, (t * NE + e) * CHUNKS + q + 1)
                part = bass.ds(e * N + q * S, S)
                nc.vector.scalar_tensor_tensor(out=gx_lo[:, part], in0=x_full[:, bass.ds(t * N + q * S, S)],
                                               scalar=coef[:, bass.ds(e * B + t * BATCHES + q, 1)],
                                               in1=gx_hi[:, part], op0=ALU.mult,
                                               op1=ALU.subtract).then_inc(gx_lo_ready, 1)

            def weight_lo(e, third):
                part = bass.ds(e * W_COLS + third * F, F)
                dve.wait_ge(w_hi_ready, 2 * e + third + 1)
                nc.vector.scalar_tensor_tensor(out=w_lo[:, part], in0=w_full[:, part], scalar=W_SCALE,
                                               in1=w_hi[:, part], op0=ALU.mult,
                                               op1=ALU.subtract).then_inc(w_lo_ready, 1)

            def hidden_of(n, f, early):
                dve.wait_ge(silu_ready, n + 1)
                if not early:
                    dve.wait_ge(h_lo_ready, n - 1)
                dve.wait_ge(up_done, n + 1)
                nc.vector.scalar_tensor_tensor(out=cols(hidden, f % 2, N), in0=cols(silu, f % 2, N),
                                               scalar=HIDDEN_RESCALE, in1=up_ps[f % 2][:, :], op0=ALU.mult,
                                               op1=ALU.mult).then_inc(hidden_ready, 1)

            def hidden_lo(n, f):
                dve.wait_ge(h_hi_ready, n + 1)
                nc.vector.tensor_tensor(cols(h_lo, f, N), cols(hidden, f % 2, N), cols(h_hi, f, N),
                                        ALU.subtract).then_inc(h_lo_ready, 1)

            def moe_out(t):
                dve.wait_ge(down_done, PER_TILE * (t + 1))
                nc.vector.scalar_tensor_tensor(out=x2T[:, :], in0=moe_ps[:, :], scalar=OUT_RESCALE,
                                               in1=cols(x_full, t, N), op0=ALU.mult,
                                               op1=ALU.add).then_inc(x2T_ready, 1)

            def norm_stats(t, q):
                done = t * BATCHES + q + 1
                if isinstance(q, int) and q == 0 or not isinstance(q, int):
                    dve.wait_ge(back_done, t + 1)
                    dve.wait_ge(x2_ready, t + 1)
                nc.vector.tensor_tensor(cols(y, q, D), cols(back_ps, q, D), cols(x2, q, D),
                                        ALU.add).then_inc(y_ready, 1)
                dve.wait_ge(y_ready, done)
                nc.vector.bn_stats(cols(stats, q, 6), cols(y, q, D)).then_inc(stats_ready, 1)

            def norm_moments(t):
                half = stats[:, :].rearrange("p (q s) -> p q s", s=6)
                mean_even, dev_even, mean_odd, dev_odd = half[:, :, 1], half[:, :, 2], half[:, :, 4], half[:, :, 5]
                dve.wait_ge(stats_ready, BATCHES * (t + 1))
                nc.vector.tensor_tensor(mean_sum[:, :], mean_even, mean_odd, ALU.add).then_inc(halves_ready, 1)
                nc.vector.tensor_tensor(mean_diff[:, :], mean_even, mean_odd, ALU.subtract).then_inc(halves_ready, 1)
                nc.vector.scalar_tensor_tensor(out=dev_sum[:, :], in0=dev_even, scalar=D * LN_EPS, in1=dev_odd,
                                               op0=ALU.add, op1=ALU.add).then_inc(halves_ready, 1)
                dve.wait_ge(halves_ready, 3 * (t + 1))
                nc.vector.tensor_scalar(mean[:, :], mean_sum[:, :], 0.5, None, ALU.mult).then_inc(mean_ready, 1)
                nc.vector.scalar_tensor_tensor(out=between[:, :], in0=mean_diff[:, :], scalar=0.25,
                                               in1=mean_diff[:, :], op0=ALU.mult,
                                               op1=ALU.mult).then_inc(between_ready, 1)
                dve.wait_ge(between_ready, t + 1)
                nc.vector.scalar_tensor_tensor(out=var_eps[:, :], in0=dev_sum[:, :], scalar=1.0 / D,
                                               in1=between[:, :], op0=ALU.mult,
                                               op1=ALU.add).then_inc(var_eps_ready, 1)

            def norm_scaled(t, q, y_q):
                gamma = affine_sb[:, bass.ds((t * BATCHES + q) * 2 * D, D)]
                nc.vector.scalar_tensor_tensor(out=cols(scaled, q, D), in0=y_q,
                                               scalar=mean[:, bass.ds(q, 1)], in1=gamma,
                                               op0=ALU.subtract, op1=ALU.mult).then_inc(scaled_ready, 1)

            def norm_result(t, q, x2_beta_q):
                dve.wait_ge(rstd_ready, t + 1)
                dve.wait_ge(scaled_ready, t * BATCHES + q + 1)
                nc.vector.scalar_tensor_tensor(out=cols(result, t * BATCHES + q, D), in0=cols(scaled, q, D),
                                               scalar=rstd[:, bass.ds(q, 1)], in1=x2_beta_q,
                                               op0=ALU.mult, op1=ALU.add).then_inc(result_ready, 1)

            def norm_out(t, q):
                dve.wait_ge(affine_loaded, 16 * B)
                dve.wait_ge(mean_ready, t + 1)
                norm_scaled(t, q, cols(y, q, D))
                dve.wait_ge(x2_beta_ready, t + 1)
                norm_result(t, q, cols(x2_beta, q, D))

            def expert(t, e, first_tile, next_w, next_gx, evacuate=None, extra=None, extra_at=CHUNKS - 1):
                for f in range(CHUNKS):
                    n = t * PER_TILE + e * CHUNKS + f
                    at_start = first_tile and isinstance(e, int) and e == 0
                    hidden_of(n, f, at_start and f < 2)
                    if evacuate is not None and f == LAG - 1:
                        moe_out(evacuate)
                    if not (at_start and f == 0):
                        hidden_lo(n - 1, (f - 1) % CHUNKS)
                    if next_w is not None and f < 2:
                        weight_lo(next_w, f)
                    if next_gx is not None:
                        for q in GATED_AT[f]:
                            gated_x_lo(next_gx[0], next_gx[1], q)
                    if extra is not None and f == extra_at:
                        extra()

            nc.vector.memset(warm[:, :], 0.0).then_inc(warm_ready, 1)
            nc.vector.memset(adapt_h[A:A + 1, :], 1.0).then_inc(ones_ready, 1)
            dve.wait_ge(x_hi_ready, 1)
            nc.vector.tensor_tensor(x_lo[:, 0:N], x_full[:, 0:N], x_hi[:, 0:N], ALU.subtract).then_inc(x_lo_ready, 1)
            weight_lo(0, 0)
            dve.wait_ge(coef_ready, 1)
            for q in range(BATCHES):
                gated_x_lo(0, 0, q)
            weight_lo(0, 1)
            for q in range(BATCHES):
                gated_x_lo(0, 1, q)
            expert(0, 0, True, 1, None)
            with dve.Fori(1, NE - 1) as e:
                expert(0, e, True, e + 1, (0, e + 1))
            expert(0, NE - 1, True, None, (1, 0))

            def tile(t, last_tile):
                expert(t, 0, False, None, (t, 1), evacuate=t - 1)
                with dve.Fori(1, 1 + BATCHES) as e:
                    expert(t, e, False, None, (t, e + 1), extra=lambda: norm_stats(t - 1, e - 1))
                norm_moments(t - 1)
                with dve.Fori(1 + BATCHES, NE - 1) as e:
                    expert(t, e, False, None, (t, e + 1),
                           extra=lambda: norm_out(t - 1, e - 1 - BATCHES))
                expert(t, NE - 1, False, None, None if last_tile else (t + 1, 0),
                       extra=lambda: norm_out(t - 1, BATCHES - 1), extra_at=1)

            with dve.Fori(1, TILES - 1) as t:
                tile(t, False)
            tile(TILES - 1, True)
            hidden_lo(TILES * PER_TILE - 1, CHUNKS - 1)
            last_tile = TILES - 1
            dve.wait_ge(down_done, PER_TILE * TILES)
            for q in range(BATCHES):
                nc.vector.scalar_tensor_tensor(out=cols(x2T, q, S), in0=cols(moe_ps, q, S), scalar=OUT_RESCALE,
                                               in1=cols(x_full, last_tile * BATCHES + q, S), op0=ALU.mult,
                                               op1=ALU.add).then_inc(x2T_ready, 1)
            for q in range(BATCHES):
                dve.wait_ge(back_done, last_tile + q + 1)
                nc.vector.bn_stats(cols(stats, q, 6), tail_y_ps[q][:, 0:D]).then_inc(stats_ready, 1)
            norm_moments(last_tile)
            dve.wait_ge(mean_ready, TILES)
            for q in range(BATCHES):
                norm_scaled(last_tile, q, tail_y_ps[q][:, 0:D])
            dve.wait_ge(x2_transposed, TILES)
            for q in range(BATCHES):
                norm_result(last_tile, q, cols(x2_ps, q, D))

        @block.gpsimd
        def _(pool):
            nc.gpsimd.memset(w_scale[:, :], W_SCALE).then_inc(w_scale_ready, 1)
            pool.wait_ge(gates_loaded, 16)
            shared_in = gates_in[:, B * (NE - 1):]
            nc.gpsimd.tensor_scalar(rest[:, :], shared_in, -X_SCALE, X_SCALE, ALU.mult,
                                    ALU.add).then_inc(rest_ready, 1)
            nc.gpsimd.tensor_scalar(coef[:, (NE - 1) * B:], shared_in, X_SCALE, None, ALU.mult)
            pool.wait_ge(rest_ready, 1)
            per_expert = coef[:, 0:(NE - 1) * B].rearrange("p (e b) -> p e b", b=B)
            nc.gpsimd.tensor_tensor(per_expert, gates_in[:, 0:B * (NE - 1)].rearrange("p (b e) -> p e b", b=B),
                                    rest[:, :].rearrange("p (o b) -> p o b", o=1).to_broadcast([P, NE - 1, B]),
                                    ALU.mult).then_inc(coef_ready, 1)

            def down_weight_parts(e):
                part = bass.ds(e * W_COLS + 2 * F, F)
                nc.gpsimd.tensor_tensor(down64[:, :], w_full[:, part], w_scale[:, :], ALU.mult).then_inc(down64_ready, 1)
                pool.wait_ge(down64_ready, e + 1)
                nc.gpsimd.tensor_copy(w_hi[:, part], down64[:, :]).then_inc(down_hi_ready, 1)
                pool.wait_ge(down_hi_ready, e + 1)
                nc.gpsimd.tensor_tensor(w_lo[:, part], down64[:, :], w_hi[:, part],
                                        ALU.subtract).then_inc(w_down_ready, 1)

            pool.wait_ge(w_scale_ready, 1)
            pool.wait_ge(w0_loaded[2], 16)
            down_weight_parts(0)
            with pool.Fori(1, NE) as e:
                pool.wait_ge(experts_loaded, e)
                pool.wait_ge(w_down_ready, e)
                down_weight_parts(e)
            pool.wait_ge(x_rest_loaded, 16)
            for t in range(1, TILES):
                nc.gpsimd.tensor_copy(cols(x_hi, t, N), cols(x_full, t, N)).then_inc(x_rest_hi_ready, 1)
                pool.wait_ge(x_rest_hi_ready, t)
                nc.gpsimd.tensor_tensor(cols(x_lo, t, N), cols(x_full, t, N), cols(x_hi, t, N),
                                        ALU.subtract).then_inc(x_rest_ready, 1)
            nc.gpsimd.memset(ident[:, :], 0.0).then_inc(ident_zeroed, 1)
            nc.gpsimd.memset(minus_half[:, :], -0.5).then_inc(ident_zeroed, 1)
            pool.wait_ge(ident_zeroed, 2)
            nc.gpsimd.affine_select(out=ident[:, :], in_=ident[:, :], compare_op=ALU.not_equal, fill=1.0, base=0,
                                    pattern=[[-1, P]], channel_multiplier=1).then_inc(consts_ready, 1)
            affine_v = affine_sb[:, :].rearrange("p (q two h) -> p q two h", two=2, h=D)
            x2_v = x2[:, :].rearrange("p (q h) -> p q h", h=D)
            x2_beta_v = x2_beta[:, :].rearrange("p (q h) -> p q h", h=D)
            pool.wait_ge(affine_loaded, 16 * B)
            for t in range(TILES):
                if t < TILES - 1:
                    pool.wait_ge(x2_ready, t + 1)
                    beta = affine_v[:, t * BATCHES:(t + 1) * BATCHES, 1]
                    nc.gpsimd.tensor_tensor(x2_beta_v, x2_v, beta, ALU.add).then_inc(x2_beta_ready, 1)
                pool.wait_ge(var_eps_ready, t + 1)
                nc.gpsimd.tensor_tensor(rstd[:, :], var_eps[:, :], minus_half[:, :], ALU.pow).then_inc(rstd_ready, 1)


_OUT = "out_dram"


def kernel(**inputs):
    import numpy as np
    import concourse.bacc as bacc
    from concourse.bass_utils import run_bass_kernel_spmd

    a = {name: np.asarray(value) for name, value in inputs.items()}
    wg = np.concatenate([a["L0_cond_Wg"], a["L0_cond_Sg"][None]])
    wu = np.concatenate([a["L0_cond_Wu"], a["L0_cond_Su"][None]])
    wd = np.concatenate([a["L0_cond_Wd"], a["L0_cond_Sd"][None]])
    wd = wd.reshape(NE, CHUNKS, P, D).transpose(0, 2, 1, 3).reshape(NE, P, F)
    arrays = {
        "xT": a["x"].reshape(TILES, N, D).transpose(0, 2, 1),
        "weights": np.concatenate([wg, wu, wd], axis=2),
        "gates": np.concatenate([a["fside_Bx8_0"].reshape(1, -1), a["condB_sharedgateprob"].reshape(1, B)], axis=1),
        "language": a["itok_B_0_8"].reshape(1, B),
        "w1": a["L1_cond_W1"],
        "w2b2": np.concatenate([a["L1_cond_W2"], a["L1_cond_b2"][:, None]], axis=1),
        "b1": a["L1_cond_b1"][:, :, None],
        "affine": np.concatenate([a["L1_cond_gamma"], a["L1_cond_beta"]], axis=1),
    }
    nc = bacc.Bacc("TRN2", target_bir_lowering=False, num_devices=1)
    args = []
    for name in list(arrays):
        arrays[name] = np.ascontiguousarray(arrays[name])
        args.append(nc.dram_tensor(name, arrays[name].shape, mybir.dt.from_np(arrays[name].dtype),
                                   kind="ExternalInput").ap())
    out = nc.dram_tensor(_OUT, (TILES, S, BATCHES, D), F32, kind="ExternalOutput").ap()
    build(nc, *args, out)
    done = run_bass_kernel_spmd(nc, [arrays], core_ids=[0])
    return done.results[0][_OUT].transpose(0, 2, 1, 3).reshape(B, S, D)
```
